# Optimizing a Trainium2 kernel written in Bass

```python
import numpy as np
import jax
import jax.numpy as jnp

def _softmax(x, axis=-1):
    return jax.nn.softmax(x, axis=axis)

def _gelu(x):
    return jax.nn.gelu(x, approximate=True)

def _silu(x):
    return jax.nn.silu(x)

def _sigmoid(x):
    return jax.nn.sigmoid(x)

def _layernorm(x, axis=-1, eps=1e-05):
    m = jnp.mean(x, axis=axis, keepdims=True)
    v = jnp.var(x, axis=axis, keepdims=True)
    return (x - m) / jnp.sqrt(v + eps)

def _scatter_add(tgt, idx, src, axis=0):
    return tgt.at[idx].add(src)

def _segment_sum(src, seg, n):
    return jax.ops.segment_sum(src, seg, n)
kernel_name = 'mk_dlrm_tower_d1_rec_r8_bf24d7'

def setup_inputs(seed: int=0):
    np.random.seed(seed)
    _w = jnp.asarray

    def _rec_inputs():
        import jax
        import jax.numpy as jnp
        _tk = jax.random.key(seed)
        ids = jnp.stack([jax.random.randint(jax.random.fold_in(_tk, 200 + f), (512,), 0, v, jnp.int32) for f, v in enumerate([1000, 12500, 1250, 1250, 1250, 1250, 1000, 12500, 1000, 1250, 1000, 1000, 12500, 125000, 12500, 1000, 12500, 1000, 12500, 12500, 1000, 1000, 12500, 1000, 1000, 1250])], axis=1)
        tbl_0 = 0.05 * jax.random.normal(jax.random.fold_in(_tk, 500 + 0), (1000, 128), jnp.float32)
        tbl_1 = 0.05 * jax.random.normal(jax.random.fold_in(_tk, 500 + 1), (12500, 128), jnp.float32)
        tbl_2 = 0.05 * jax.random.normal(jax.random.fold_in(_tk, 500 + 2), (1250, 128), jnp.float32)
        tbl_3 = 0.05 * jax.random.normal(jax.random.fold_in(_tk, 500 + 3), (1250, 128), jnp.float32)
        tbl_4 = 0.05 * jax.random.normal(jax.random.fold_in(_tk, 500 + 4), (1250, 128), jnp.float32)
        tbl_5 = 0.05 * jax.random.normal(jax.random.fold_in(_tk, 500 + 5), (1250, 128), jnp.float32)
        tbl_6 = 0.05 * jax.random.normal(jax.random.fold_in(_tk, 500 + 6), (1000, 128), jnp.float32)
        tbl_7 = 0.05 * jax.random.normal(jax.random.fold_in(_tk, 500 + 7), (12500, 128), jnp.float32)
        tbl_8 = 0.05 * jax.random.normal(jax.random.fold_in(_tk, 500 + 8), (1000, 128), jnp.float32)
        tbl_9 = 0.05 * jax.random.normal(jax.random.fold_in(_tk, 500 + 9), (1250, 128), jnp.float32)
        tbl_10 = 0.05 * jax.random.normal(jax.random.fold_in(_tk, 500 + 10), (1000, 128), jnp.float32)
        tbl_11 = 0.05 * jax.random.normal(jax.random.fold_in(_tk, 500 + 11), (1000, 128), jnp.float32)
        tbl_12 = 0.05 * jax.random.normal(jax.random.fold_in(_tk, 500 + 12), (12500, 128), jnp.float32)
        tbl_13 = 0.05 * jax.random.normal(jax.random.fold_in(_tk, 500 + 13), (125000, 128), jnp.float32)
        tbl_14 = 0.05 * jax.random.normal(jax.random.fold_in(_tk, 500 + 14), (12500, 128), jnp.float32)
        tbl_15 = 0.05 * jax.random.normal(jax.random.fold_in(_tk, 500 + 15), (1000, 128), jnp.float32)
        tbl_16 = 0.05 * jax.random.normal(jax.random.fold_in(_tk, 500 + 16), (12500, 128), jnp.float32)
        tbl_17 = 0.05 * jax.random.normal(jax.random.fold_in(_tk, 500 + 17), (1000, 128), jnp.float32)
        tbl_18 = 0.05 * jax.random.normal(jax.random.fold_in(_tk, 500 + 18), (12500, 128), jnp.float32)
        tbl_19 = 0.05 * jax.random.normal(jax.random.fold_in(_tk, 500 + 19), (12500, 128), jnp.float32)
        tbl_20 = 0.05 * jax.random.normal(jax.random.fold_in(_tk, 500 + 20), (1000, 128), jnp.float32)
        tbl_21 = 0.05 * jax.random.normal(jax.random.fold_in(_tk, 500 + 21), (1000, 128), jnp.float32)
        tbl_22 = 0.05 * jax.random.normal(jax.random.fold_in(_tk, 500 + 22), (12500, 128), jnp.float32)
        tbl_23 = 0.05 * jax.random.normal(jax.random.fold_in(_tk, 500 + 23), (1000, 128), jnp.float32)
        tbl_24 = 0.05 * jax.random.normal(jax.random.fold_in(_tk, 500 + 24), (1000, 128), jnp.float32)
        tbl_25 = 0.05 * jax.random.normal(jax.random.fold_in(_tk, 500 + 25), (1250, 128), jnp.float32)
        _rk = jax.random.fold_in(_tk, 7)
        r_dense_features = -0.000520686 + 1.00062 * jax.random.normal(jax.random.fold_in(_rk, 101), (512, 128), jnp.float32)
        W_top1 = 0.0405887 * jax.random.normal(jax.random.fold_in(_tk, 801), (607, 512), jnp.float32)
        W_top2 = 0.0441942 * jax.random.normal(jax.random.fold_in(_tk, 802), (512, 256), jnp.float32)
        W_top3 = 0.0625 * jax.random.normal(jax.random.fold_in(_tk, 803), (256, 1), jnp.float32)
        b_top1 = jnp.zeros((512,), jnp.float32)
        b_top2 = jnp.zeros((256,), jnp.float32)
        return (r_dense_features, ids, tbl_0, tbl_1, tbl_2, tbl_3, tbl_4, tbl_5, tbl_6, tbl_7, tbl_8, tbl_9, tbl_10, tbl_11, tbl_12, tbl_13, tbl_14, tbl_15, tbl_16, tbl_17, tbl_18, tbl_19, tbl_20, tbl_21, tbl_22, tbl_23, tbl_24, tbl_25, W_top1, b_top1, W_top2, b_top2, W_top3)
    r_dense_features, ids, tbl_0, tbl_1, tbl_2, tbl_3, tbl_4, tbl_5, tbl_6, tbl_7, tbl_8, tbl_9, tbl_10, tbl_11, tbl_12, tbl_13, tbl_14, tbl_15, tbl_16, tbl_17, tbl_18, tbl_19, tbl_20, tbl_21, tbl_22, tbl_23, tbl_24, tbl_25, W_top1, b_top1, W_top2, b_top2, W_top3 = _rec_inputs()

    def _L0_rec_setup():
        import jax, jax.numpy as jnp
        import numpy as np
        NUM_SPARSE = 26
        EMBED_DIM = 128
        BATCH = 2048
        key = jax.random.key(seed)
        k1, k2 = jax.random.split(key)
        dense_features = jax.random.normal(k1, (BATCH, EMBED_DIM), dtype=jnp.float32)
        sparse_features = jax.random.normal(k2, (BATCH, NUM_SPARSE, EMBED_DIM), dtype=jnp.float32)
        return {'dense_features': dense_features, 'sparse_features': sparse_features}
    _L0_rec_all = _L0_rec_setup()
    _L0_rec_in = {k: v for k, v in _L0_rec_all.items() if k in ()}
    del _L0_rec_all
    return {'r_dense_features': r_dense_features, 'ids': ids, 'tbl_0': tbl_0, 'tbl_1': tbl_1, 'tbl_2': tbl_2, 'tbl_3': tbl_3, 'tbl_4': tbl_4, 'tbl_5': tbl_5, 'tbl_6': tbl_6, 'tbl_7': tbl_7, 'tbl_8': tbl_8, 'tbl_9': tbl_9, 'tbl_10': tbl_10, 'tbl_11': tbl_11, 'tbl_12': tbl_12, 'tbl_13': tbl_13, 'tbl_14': tbl_14, 'tbl_15': tbl_15, 'tbl_16': tbl_16, 'tbl_17': tbl_17, 'tbl_18': tbl_18, 'tbl_19': tbl_19, 'tbl_20': tbl_20, 'tbl_21': tbl_21, 'tbl_22': tbl_22, 'tbl_23': tbl_23, 'tbl_24': tbl_24, 'tbl_25': tbl_25, 'W_top1': W_top1, 'b_top1': b_top1, 'W_top2': W_top2, 'b_top2': b_top2, 'W_top3': W_top3}

def reference(r_dense_features, ids, tbl_0, tbl_1, tbl_2, tbl_3, tbl_4, tbl_5, tbl_6, tbl_7, tbl_8, tbl_9, tbl_10, tbl_11, tbl_12, tbl_13, tbl_14, tbl_15, tbl_16, tbl_17, tbl_18, tbl_19, tbl_20, tbl_21, tbl_22, tbl_23, tbl_24, tbl_25, W_top1, b_top1, W_top2, b_top2, W_top3):
    import jax
    import jax.numpy as jnp

    def _L0_rec_ref(dense_features, sparse_features):
        import jax, jax.numpy as jnp
        import numpy as np
        NUM_SPARSE = 26
        EMBED_DIM = 128
        BATCH = 2048
        F = NUM_SPARSE + 1
        combined = jnp.concatenate([dense_features[:, None, :], sparse_features], axis=1)
        interactions = jnp.einsum('bfd,bgd->bfg', combined, combined)
        iu, ju = jnp.triu_indices(F, k=1)
        interactions_flat = interactions[:, iu, ju]
        return jnp.concatenate([dense_features, interactions_flat], axis=1)
    e = jnp.stack([tbl_0[ids[:, 0]], tbl_1[ids[:, 1]], tbl_2[ids[:, 2]], tbl_3[ids[:, 3]], tbl_4[ids[:, 4]], tbl_5[ids[:, 5]], tbl_6[ids[:, 6]], tbl_7[ids[:, 7]], tbl_8[ids[:, 8]], tbl_9[ids[:, 9]], tbl_10[ids[:, 10]], tbl_11[ids[:, 11]], tbl_12[ids[:, 12]], tbl_13[ids[:, 13]], tbl_14[ids[:, 14]], tbl_15[ids[:, 15]], tbl_16[ids[:, 16]], tbl_17[ids[:, 17]], tbl_18[ids[:, 18]], tbl_19[ids[:, 19]], tbl_20[ids[:, 20]], tbl_21[ids[:, 21]], tbl_22[ids[:, 22]], tbl_23[ids[:, 23]], tbl_24[ids[:, 24]], tbl_25[ids[:, 25]]], axis=1)
    z = _L0_rec_ref(r_dense_features, e)
    z = z.reshape(z.shape[0], -1)
    h = jnp.concatenate([z, r_dense_features], axis=1)
    h = jnp.maximum(h @ W_top1 + b_top1, 0.0)
    h = jnp.maximum(h @ W_top2 + b_top2, 0.0)
    y = h @ W_top3
    return y

_drawn_inputs = setup_inputs


def setup_inputs(seed=0):
    import zlib

    import numpy as np

    out = dict(_drawn_inputs(seed))
    spreads = {'b_top1': (0.0, 0.1), 'b_top2': (0.0, 0.1)}
    factors = {}
    for name, (base, spread) in spreads.items():
        noise = np.random.default_rng([zlib.crc32(name.encode()), seed]).standard_normal(out[name].shape)
        drawn = base * np.exp(spread * noise) if base else spread * noise
        out[name] = jnp.asarray(drawn.astype(out[name].dtype))
    for name, factor in factors.items():
        out[name] = (out[name] * factor).astype(out[name].dtype)
    return out
```

```python
from contextlib import ExitStack

import concourse.bass as bass
from concourse import mybir

F32 = mybir.dt.float32
I32 = mybir.dt.int32
ALU = mybir.AluOpType
ACT = mybir.ActivationFunctionType

P = 128
QUAD = 32
SLOTS_PER_BANK = 4
GROUP = P // QUAD
GROUPS_PER_BANK = 4
BLOCK_BANKS = 2
BLOCK = GROUPS_PER_BANK * BLOCK_BANKS


def dlrm_tower(nc, dense, ids, tables, w_pairs, w_dense, b1, w2, b2, w3, out):
    B, D = dense.shape
    NS = len(tables)
    NF = NS + 1
    ND = (NF - 1) // 2
    NW = NF + ND
    KP, KC, H1 = w_pairs.shape
    FC = NF // KC
    H2 = w2.shape[1]
    N1, N2 = H1 // P, H2 // P
    TILES = B // P
    QUARTETS = [list(range(s, min(s + SLOTS_PER_BANK, NF))) for s in range(0, NF, SLOTS_PER_BANK)]
    NQ = len(QUARTETS)
    BLOCKS = P // (GROUP * BLOCK)
    assert D == P and B % P == 0 and NF % 2 == 1 and NF <= QUAD and KP == FC * ND

    gram_dram = nc.dram_tensor("gram_dram", (NF, NW, P), F32, kind="Internal").ap()

    with ExitStack() as ctx:
        def sb(name, shape, dt=F32):
            return ctx.enter_context(nc.sbuf_tensor(name, shape, dt))

        def psum(name, shape):
            return ctx.enter_context(nc.psum_tensor(name, shape, F32))

        def sem(name):
            return ctx.enter_context(nc.semaphore(name))

        ids_all = sb("ids_all", [P, TILES, NS], I32)
        ids_tile = sb("ids_tile", [P, NS], I32)
        rows = sb("rows", [P, NF, D])
        feat_t = sb("feat_t", [P, P, QUAD])
        dense_t = sb("dense_t", [P, P])
        identity = sb("identity", [P, P])
        gram = sb("gram", [NF, NF, P])
        pairs = sb("pairs", [KP, KC, P])
        w_pairs_sb = sb("w_pairs_sb", [KP, KC, H1])
        w_dense_sb = sb("w_dense_sb", [P, 2, H1])
        w_dense_sum = sb("w_dense_sum", [P, H1])
        w2_sb = sb("w2_sb", [P, N1, H2])
        w3_sb = sb("w3_sb", [P, N2])
        b1_sb = sb("b1_sb", [P, N1])
        b2_sb = sb("b2_sb", [P, N2])
        h1 = sb("h1", [P, N1, P])
        h2 = sb("h2", [P, N2, P])
        y_all = sb("y_all", [1, B])

        transposed_ps = [psum(f"transposed_ps{i}", [P, SLOTS_PER_BANK, P]) for i in range(2)]
        gram_ps = [psum(f"gram_ps{i}", [P, BLOCK_BANKS, 512]) for i in range(2)]
        h1_ps = psum("h1_ps", [P, N1, P])
        h2_ps = psum("h2_ps", [P, N2 + 1, P])

        ids_loaded = sem("ids_loaded")
        dense_loaded = sem("dense_loaded")
        weights_loaded = sem("weights_loaded")
        identity_zeroed = sem("identity_zeroed")
        identity_made = sem("identity_made")
        ids_copied = sem("ids_copied")
        quartets_begun = sem("quartets_begun")
        gathered = [sem(f"gathered{f}") for f in range(NS)]
        transposed = [sem(f"transposed{q}") for q in range(NQ)]
        evacuated = sem("evacuated")
        pads_zeroed = sem("pads_zeroed")
        weights_summed = sem("weights_summed")
        dense_t_made = sem("dense_t_made")
        gram_done = sem("gram_done")
        gram_copied = sem("gram_copied")
        gram_written = sem("gram_written")
        pairs_read = sem("pairs_read")
        layer1_done = sem("layer1_done")
        layer2_done = sem("layer2_done")
        layer3_done = sem("layer3_done")
        h1_made = sem("h1_made")
        h2_made = sem("h2_made")
        y_made = sem("y_made")
        out_written = sem("out_written")

        def wait_after_first(engine, semaphore, count):
            if not isinstance(count, int) or count > 0:
                engine.wait_ge(semaphore, count)

        block = ctx.enter_context(nc.Block())
        N_WEIGHT_DMAS = 6

        @block.sync
        def _(sp):
            def load_dense(t):
                wait_after_first(sp, transposed[0], t)
                sp.dma_start(rows[:, 0, :], dense[bass.ds(t * P, P), :]).then_inc(dense_loaded, 16)

            def regroup_pairs(t):
                sp.wait_ge(gram_copied, BLOCKS * (t + 1))
                sp.dma_start(gram_dram[:, 0:NF, :], gram[:, :, :]).then_inc(gram_written, 16)
                sp.dma_start(gram_dram[:, NF:NW, :], gram[:, 0:ND, :]).then_inc(gram_written, 16)
                sp.wait_ge(gram_written, 32 * (t + 1))
                wait_after_first(sp, layer1_done, t)
                for c in range(KC):
                    src = bass.AP(tensor=gram_dram.tensor, offset=gram_dram.offset + (c * FC * (NW + 1) + 1) * P,
                                  ap=[[(NW + 1) * P, FC], [P, ND], [1, P]])
                    sp.dma_start(pairs[:, c, :], src).then_inc(pairs_read, 16)

            sp.dma_start(ids_all[:], ids.rearrange("(t p) f -> p t f", p=P)).then_inc(ids_loaded, 16)
            load_dense(0)
            sp.dma_start(w_pairs_sb[:], w_pairs).then_inc(weights_loaded, 16)
            sp.dma_start(w_dense_sb[:], w_dense).then_inc(weights_loaded, 16)
            sp.dma_start(w2_sb[:], w2.rearrange("(c p) n -> p c n", p=P)).then_inc(weights_loaded, 16)
            sp.dma_start(w3_sb[:], w3).then_inc(weights_loaded, 16)
            sp.dma_start(b1_sb[:], b1).then_inc(weights_loaded, 16)
            sp.dma_start(b2_sb[:], b2).then_inc(weights_loaded, 16)
            load_dense(1)
            regroup_pairs(0)
            with sp.Fori(1, TILES - 1) as t:
                load_dense(t + 1)
                regroup_pairs(t)
            regroup_pairs(TILES - 1)
            sp.wait_ge(y_made, TILES)
            sp.dma_start(out, y_all[:]).then_inc(out_written, 16)
            sp.wait_ge(out_written, 16)

        @block.gpsimd
        def _(pool):
            def gather_tile(t):
                for q, slots in enumerate(QUARTETS):
                    sparse = [slot - 1 for slot in slots if slot > 0]
                    fs = slice(sparse[0], sparse[-1] + 1)
                    wait_after_first(pool, transposed[q], t)
                    pool.tensor_copy(ids_tile[:, fs], ids_all[:, bass.ds(t, 1), fs]).then_inc(ids_copied, 1)
                    pool.wait_ge(ids_copied, NQ * t + q + 1)
                    pool.sem_inc(quartets_begun, 1)
                    for f in sparse:
                        pool.indirect_dma_start(
                            rows[:, f + 1, :], None, tables[f],
                            bass.IndirectOffsetOnAxis(ap=ids_tile[:, f:f + 1], axis=0)).then_inc(gathered[f], 16)

            pool.memset(identity[:], 0.0).then_inc(identity_zeroed, 1)
            pool.wait_ge(identity_zeroed, 1)
            pool.affine_select(out=identity[:], in_=identity[:], compare_op=ALU.not_equal, fill=1.0, base=0,
                               pattern=[[-1, P]], channel_multiplier=1).then_inc(identity_made, 1)
            pool.wait_ge(ids_loaded, 16)
            gather_tile(0)
            with pool.Fori(1, TILES) as t:
                gather_tile(t)

        @block.tensor
        def _(pe):
            def transpose_quartet(t, q):
                wait_after_first(pe, evacuated, NQ * t + max(q - 1, 0))
                for i, slot in enumerate(QUARTETS[q]):
                    if slot == 0:
                        pe.wait_ge(dense_loaded, 16 * (t + 1))
                    else:
                        pe.wait_ge(gathered[slot - 1], 16 * (t + 1))
                    last = nc.tensor.transpose(transposed_ps[q % 2][:, i, :], rows[:, slot, :], identity[:])
                last.then_inc(transposed[q], 1)

            def gram_block(t, k):
                wait_after_first(pe, gram_copied, BLOCKS * t + max(k - 1, 0))
                for i in range(BLOCK):
                    s = GROUP * (BLOCK * k + i)
                    bank, r = divmod(i, GROUPS_PER_BANK)
                    last = nc.tensor.matmul(
                        gram_ps[k % 2][:, bank, r * GROUP * NF:(r + 1) * GROUP * NF],
                        feat_t[:, s:s + GROUP, :], feat_t[:, s:s + GROUP, 0:NF], start=True, stop=True)
                last.then_inc(gram_done, 1)

            def layers(t):
                pe.wait_ge(pairs_read, 16 * KC * (t + 1))
                pe.wait_ge(dense_t_made, t + 1)
                for n in range(N1):
                    cols = slice(n * P, (n + 1) * P)
                    nc.tensor.matmul(h1_ps[:, n, :], w_dense_sum[:, cols], dense_t[:], start=True, stop=False)
                    for c in range(KC):
                        last = nc.tensor.matmul(h1_ps[:, n, :], w_pairs_sb[:, c, cols], pairs[:, c, :],
                                                start=False, stop=c == KC - 1)
                last.then_inc(layer1_done, 1)
                pe.wait_ge(h1_made, t + 1)
                for m in range(N2):
                    for n in range(N1):
                        last = nc.tensor.matmul(h2_ps[:, m, :], w2_sb[:, n, m * P:(m + 1) * P], h1[:, n, :],
                                                start=n == 0, stop=n == N1 - 1)
                last.then_inc(layer2_done, 1)
                pe.wait_ge(h2_made, t + 1)
                for m in range(N2):
                    last = nc.tensor.matmul(h2_ps[0:1, N2, :], w3_sb[:, m:m + 1], h2[:, m, :],
                                            start=m == 0, stop=m == N2 - 1)
                last.then_inc(layer3_done, 1)

            def gram_blocks(t):
                pe.wait_ge(evacuated, NQ * (t + 1))
                for k in range(BLOCKS):
                    gram_block(t, k)

            pe.wait_ge(identity_made, 1)
            pe.wait_ge(pads_zeroed, 1)
            for q in range(NQ):
                transpose_quartet(0, q)
            gram_blocks(0)
            pe.wait_ge(weights_loaded, 16 * N_WEIGHT_DMAS)
            pe.wait_ge(weights_summed, 1)
            with pe.Fori(1, TILES) as t:
                transpose_quartet(t, 0)
                transpose_quartet(t, 1)
                layers(t - 1)
                for q in range(2, NQ):
                    transpose_quartet(t, q)
                gram_blocks(t)
            layers(TILES - 1)

        @block.vector
        def _(dve):
            def assemble_tile(t):
                wait_after_first(dve, gram_done, BLOCKS * t)
                wait_after_first(dve, dense_t_made, t)
                for q, slots in enumerate(QUARTETS):
                    dve.wait_ge(transposed[q], t + 1)
                    dve.tensor_copy(feat_t[:, :, slots[0]:slots[-1] + 1].rearrange("d s f -> d f s"),
                                    transposed_ps[q % 2][:, 0:len(slots), :]).then_inc(evacuated, 1)
                dve.wait_ge(evacuated, NQ * t + 1)
                wait_after_first(dve, layer1_done, t)
                dve.tensor_copy(dense_t[:], feat_t[:, :, 0]).then_inc(dense_t_made, 1)

            dve.memset(feat_t[:, :, NF:QUAD], 0.0).then_inc(pads_zeroed, 1)
            dve.wait_ge(weights_loaded, 16 * N_WEIGHT_DMAS)
            dve.tensor_tensor(w_dense_sum[:], w_dense_sb[:, 0, :], w_dense_sb[:, 1, :], ALU.add).then_inc(weights_summed, 1)
            assemble_tile(0)
            with dve.Fori(1, TILES) as t:
                assemble_tile(t)

        @block.scalar
        def _(act):
            def copy_gram(t):
                wait_after_first(act, gram_written, 32 * t)
                for k in range(BLOCKS):
                    act.wait_ge(gram_done, BLOCKS * t + k + 1)
                    ps = gram_ps[k % 2][:, :, 0:GROUPS_PER_BANK * GROUP * NF].rearrange(
                        "p b (r s g) -> p b r s g", r=GROUPS_PER_BANK, s=GROUP)
                    to = gram[:, :, GROUP * BLOCK * k:GROUP * BLOCK * (k + 1)].rearrange(
                        "f g (b r s) -> f b r s g", b=BLOCK_BANKS, s=GROUP)
                    for s in range(GROUP):
                        last = nc.scalar.copy(to[:, :, :, s, :], ps[QUAD * s:QUAD * s + NF, :, :, s, :])
                    last.then_inc(gram_copied, 1)

            def activations(t):
                act.wait_ge(layer1_done, t + 1)
                for n in range(N1):
                    last = nc.scalar.activation(h1[:, n, :], h1_ps[:, n, :], ACT.Relu, bias=b1_sb[:, n:n + 1])
                last.then_inc(h1_made, 1)
                act.wait_ge(layer2_done, t + 1)
                for m in range(N2):
                    last = nc.scalar.activation(h2[:, m, :], h2_ps[:, m, :], ACT.Relu, bias=b2_sb[:, m:m + 1])
                last.then_inc(h2_made, 1)
                act.wait_ge(layer3_done, t + 1)
                nc.scalar.copy(y_all[:, bass.ds(t * P, P)], h2_ps[0:1, N2, :]).then_inc(y_made, 1)

            act.wait_ge(weights_loaded, 16 * N_WEIGHT_DMAS)
            copy_gram(0)
            with act.Fori(1, TILES) as t:
                activations(t - 1)
                copy_gram(t)
            activations(TILES - 1)


def kernel(**inputs):
    import numpy as np
    import concourse.bacc as bacc
    from concourse.bass_utils import run_bass_kernel_spmd

    ids = np.ascontiguousarray(inputs["ids"])
    dense = np.ascontiguousarray(inputs["r_dense_features"])
    B, NS = ids.shape
    D = dense.shape[1]
    NF = NS + 1
    ND = (NF - 1) // 2
    KC = 3
    first, second = np.triu_indices(NF, k=1)
    row_of = np.zeros((NF, NF), np.int64)
    row_of[first, second] = row_of[second, first] = D + np.arange(len(first))
    f = np.arange(NF)[:, None]
    order = row_of[f, (f + 1 + np.arange(ND)[None, :]) % NF].reshape(KC, -1)
    w1 = np.asarray(inputs["W_top1"])
    H1 = w1.shape[1]
    arrays = {
        "dense": dense,
        "ids": ids,
        "w_pairs": np.ascontiguousarray(w1[order].transpose(1, 0, 2)),
        "w_dense": np.ascontiguousarray(np.stack([w1[:D], w1[D + len(first):]], axis=1)),
        "b1": np.ascontiguousarray(np.asarray(inputs["b_top1"]).reshape(-1, P).T),
        "w2": np.ascontiguousarray(inputs["W_top2"]),
        "b2": np.ascontiguousarray(np.asarray(inputs["b_top2"]).reshape(-1, P).T),
        "w3": np.ascontiguousarray(np.asarray(inputs["W_top3"]).reshape(-1, P).T),
    }
    for n in range(NS):
        arrays[f"tbl_{n}"] = np.ascontiguousarray(inputs[f"tbl_{n}"])

    nc = bacc.Bacc("TRN2", target_bir_lowering=False, num_devices=1)
    ap = {n: nc.dram_tensor(n, a.shape, mybir.dt.from_np(a.dtype), kind="ExternalInput").ap()
          for n, a in arrays.items()}
    out = nc.dram_tensor("out", (1, B), F32, kind="ExternalOutput").ap()
    dlrm_tower(nc, ap["dense"], ap["ids"], [ap[f"tbl_{n}"] for n in range(NS)], ap["w_pairs"], ap["w_dense"],
               ap["b1"], ap["w2"], ap["b2"], ap["w3"], out)
    result = run_bass_kernel_spmd(nc, [arrays], core_ids=[0])
    return result.results[0]["out"].reshape(B, 1)
```

```python
from contextlib import ExitStack

import concourse.bass as bass
from concourse import mybir

F32 = mybir.dt.float32
F32R = mybir.dt.float32r
I32 = mybir.dt.int32
ALU = mybir.AluOpType
ACT = mybir.ActivationFunctionType

P = 128
QUAD = 32
SLOTS_PER_BANK = 4
GROUP = P // QUAD
GROUPS_PER_BANK = 4
BLOCK_BANKS = 2
BLOCK = GROUPS_PER_BANK * BLOCK_BANKS
PICK_CHUNKS = 8
MAX_PICKED = 8


def dlrm_tower(nc, dense, ids, pick_ids, pick_tables, tables, w_pairs, w_dense, b1, w2, b2, w3, out):
    B, D = dense.shape
    NG = len(tables)
    NP, V, _ = pick_tables.shape
    PV = V // PICK_CHUNKS
    SLOTS = 1 + NG
    NF = SLOTS + NP
    ND = (NF - 1) // 2
    NW = NF + ND
    KP, KC, H1 = w_pairs.shape
    FC = NF // KC
    H2 = w2.shape[1]
    N1, N2 = H1 // P, H2 // P
    TILES = B // P
    QUARTETS = [list(range(s, min(s + SLOTS_PER_BANK, SLOTS))) for s in range(0, SLOTS, SLOTS_PER_BANK)]
    NQ = len(QUARTETS)
    BLOCKS = P // (GROUP * BLOCK)
    assert D == P and B == 512 and NF % 2 == 1 and NF <= QUAD and KP == FC * ND
    assert V % PICK_CHUNKS == 0 and PV <= P and NP % 2 == 0 and TILES % 2 == 0

    gram_dram = [nc.dram_tensor(f"gram_dram{i}", (NF, NW, P), F32, kind="Internal").ap() for i in range(2)]

    with ExitStack() as ctx:
        def sb(name, shape, dt=F32):
            return ctx.enter_context(nc.sbuf_tensor(name, shape, dt))

        def psum(name, shape):
            return ctx.enter_context(nc.psum_tensor(name, shape, F32))

        def sem(name):
            return ctx.enter_context(nc.semaphore(name))

        table = [sb(f"table{i}", [PV, PICK_CHUNKS, D]) for i in range(2)]
        table_hi = [sb(f"table_hi{i}", [PV, PICK_CHUNKS, D], F32R) for i in range(2)]
        table_lo = [sb(f"table_lo{i}", [PV, PICK_CHUNKS, D], F32R) for i in range(2)]
        wanted = [sb(f"wanted{i}", [PV, B], I32) for i in range(2)]
        row_number = sb("row_number", [PV, PICK_CHUNKS])
        onehot = [sb(f"onehot{i}", [PV, PICK_CHUNKS, B], F32R) for i in range(2)]
        picked_t = sb("picked_t", [P, NP, B])
        ids_sb = sb("ids_sb", [P, TILES, NG], I32)
        rows = [sb(f"rows{i}", [P, SLOTS, D]) for i in range(2)]
        identity = sb("identity", [P, P])
        feat_t = sb("feat_t", [P, P, QUAD])
        dense_t = [sb(f"dense_t{i}", [P, P]) for i in range(2)]
        gram = sb("gram", [NF, NF, P])
        pairs = [sb(f"pairs{i}", [KP, KC, P]) for i in range(2)]
        w_pairs_sb = sb("w_pairs_sb", [KP, KC, H1])
        w_dense_sb = sb("w_dense_sb", [P, 2, H1])
        w_dense_sum = sb("w_dense_sum", [P, H1])
        w2_sb = sb("w2_sb", [P, N1, H2])
        w3_sb = sb("w3_sb", [P, N2])
        b1_sb = sb("b1_sb", [P, N1])
        b2_sb = sb("b2_sb", [P, N2])
        h1 = sb("h1", [P, N1, P])
        h2 = sb("h2", [P, N2, P])
        y_all = sb("y_all", [1, B])

        transposed_ps = [psum(f"transposed_ps{i}", [P, SLOTS_PER_BANK, P]) for i in range(2)]
        gram_ps = [psum(f"gram_ps{i}", [P, BLOCK_BANKS, 512]) for i in range(2)]
        h1_ps = psum("h1_ps", [P, B])
        h2_ps = psum("h2_ps", [P, B])
        picked_ps = [h1_ps, h2_ps]

        table_loaded = [sem(f"table_loaded{i}") for i in range(2)]
        wanted_loaded = [sem(f"wanted_loaded{i}") for i in range(2)]
        row_number_made = sem("row_number_made")
        hi_made = sem("hi_made")
        lo_made = sem("lo_made")
        onehot_made = sem("onehot_made")
        picked = sem("picked")
        picked_copied = sem("picked_copied")
        picked_placed = sem("picked_placed")
        ids_loaded = sem("ids_loaded")
        dense_loaded = [sem(f"dense_loaded{i}") for i in range(2)]
        weights_loaded = sem("weights_loaded")
        identity_zeroed = sem("identity_zeroed")
        identity_made = sem("identity_made")
        gathered = [[sem(f"gathered{i}_{f}") for f in range(NG)] for i in range(2)]
        transposed = [sem(f"transposed{q}") for q in range(NQ)]
        evacuated = sem("evacuated")
        pads_zeroed = sem("pads_zeroed")
        weights_summed = sem("weights_summed")
        dense_t_made = sem("dense_t_made")
        gram_done = sem("gram_done")
        gram_copied = sem("gram_copied")
        gram_written = sem("gram_written")
        pairs_read = [sem(f"pairs_read{i}") for i in range(2)]
        layer1_done = sem("layer1_done")
        layer2_done = sem("layer2_done")
        layer3_done = sem("layer3_done")
        h1_made = sem("h1_made")
        h2_made = sem("h2_made")
        y_made = sem("y_made")
        out_written = sem("out_written")

        def wait_after_first(engine, semaphore, count):
            if not isinstance(count, int) or count > 0:
                engine.wait_ge(semaphore, count)

        block = ctx.enter_context(nc.Block())
        N_WEIGHT_DMAS = 6

        @block.sync
        def _(sp):
            def load_table(kk, i):
                k = 2 * kk + i
                wait_after_first(sp, lo_made, k - 1)
                sp.dma_start(wanted[i][:], pick_ids[bass.ds(k, 1), :].to_broadcast([PV, B])).then_inc(wanted_loaded[i], 16)
                sp.dma_start(table[i][:], pick_tables[bass.ds(k, 1), :, :].rearrange(
                    "o (p c) d -> p (o c) d", c=PICK_CHUNKS)).then_inc(table_loaded[i], 16)

            def load_dense(t):
                if t > 1:
                    sp.wait_ge(transposed[0], t - 1)
                sp.dma_start(rows[t % 2][:, 0, :], dense[t * P:(t + 1) * P, :]).then_inc(dense_loaded[t % 2], 16)

            sp.dma_start(ids_sb[:], ids.rearrange("(t p) f -> p t f", p=P)).then_inc(ids_loaded, 16)
            load_table(0, 0)
            load_table(0, 1)
            load_dense(0)
            load_dense(1)
            with sp.Fori(1, NP // 2) as kk:
                load_table(kk, 0)
                load_table(kk, 1)
            sp.dma_start(w_pairs_sb[:], w_pairs).then_inc(weights_loaded, 16)
            sp.dma_start(w_dense_sb[:], w_dense).then_inc(weights_loaded, 16)
            sp.dma_start(w2_sb[:], w2.rearrange("(c p) n -> p c n", p=P)).then_inc(weights_loaded, 16)
            sp.dma_start(w3_sb[:], w3).then_inc(weights_loaded, 16)
            sp.dma_start(b1_sb[:], b1).then_inc(weights_loaded, 16)
            sp.dma_start(b2_sb[:], b2).then_inc(weights_loaded, 16)
            for t in range(TILES):
                i = t % 2
                sp.wait_ge(gram_copied, BLOCKS * (t + 1))
                sp.dma_start(gram_dram[i][:, 0:NF, :], gram[:, :, :]).then_inc(gram_written, 16)
                sp.dma_start(gram_dram[i][:, NF:NW, :], gram[:, 0:ND, :]).then_inc(gram_written, 16)
                if t + 2 < TILES:
                    load_dense(t + 2)
                sp.wait_ge(gram_written, 32 * (t + 1))
                for c in range(KC):
                    src = bass.AP(tensor=gram_dram[i].tensor, offset=gram_dram[i].offset + (c * FC * (NW + 1) + 1) * P,
                                  ap=[[(NW + 1) * P, FC], [P, ND], [1, P]])
                    sp.dma_start(pairs[i][:, c, :], src).then_inc(pairs_read[i], 16)
            sp.wait_ge(y_made, TILES)
            sp.dma_start(out, y_all[:]).then_inc(out_written, 16)
            sp.wait_ge(out_written, 16)

        @block.gpsimd
        def _(pool):
            pool.iota(row_number[:], [[1, PICK_CHUNKS]], base=0, channel_multiplier=PICK_CHUNKS,
                      allow_small_or_imprecise_dtypes=True).then_inc(row_number_made, 1)
            pool.memset(identity[:], 0.0).then_inc(identity_zeroed, 1)
            pool.wait_ge(identity_zeroed, 1)
            pool.affine_select(out=identity[:], in_=identity[:], compare_op=ALU.not_equal, fill=1.0, base=0,
                               pattern=[[-1, P]], channel_multiplier=1).then_inc(identity_made, 1)
            pool.wait_ge(ids_loaded, 16)
            for t in range(TILES):
                for f in range(NG):
                    q = (f + 1) // SLOTS_PER_BANK
                    if t > 1 and (f == 0 or (f + 1) % SLOTS_PER_BANK == 0):
                        pool.wait_ge(transposed[q], t - 1)
                    pool.indirect_dma_start(
                        rows[t % 2][:, f + 1, :], None, tables[f],
                        bass.IndirectOffsetOnAxis(ap=ids_sb[:, t, f:f + 1], axis=0)).then_inc(gathered[t % 2][f], 16)

        @block.tensor
        def _(pe):
            def pick(kk, i):
                k = 2 * kk + i
                wait_after_first(pe, picked_copied, k - 1)
                pe.wait_ge(hi_made, k + 1)
                for c in range(PICK_CHUNKS):
                    pe.wait_ge(onehot_made, PICK_CHUNKS * k + c + 1)
                    nc.tensor.matmul(picked_ps[i][:], table_hi[i][:, c, :], onehot[i][:, c, :], start=c == 0, stop=False)
                pe.wait_ge(lo_made, k + 1)
                for c in range(PICK_CHUNKS):
                    last = nc.tensor.matmul(picked_ps[i][:], table_lo[i][:, c, :], onehot[i][:, c, :],
                                            start=False, stop=c == PICK_CHUNKS - 1)
                last.then_inc(picked, 1)

            def transpose_quartet(j, i, q):
                if q > 1:
                    pe.wait_ge(evacuated, NQ * (2 * j + i) + q - 1)
                for n, slot in enumerate(QUARTETS[q]):
                    if slot == 0:
                        pe.wait_ge(dense_loaded[i], 16 * (j + 1))
                    else:
                        pe.wait_ge(gathered[i][slot - 1], 16 * (j + 1))
                    last = nc.tensor.transpose(transposed_ps[q % 2][:, n, :], rows[i][:, slot, :], identity[:])
                last.then_inc(transposed[q], 1)

            def gram_products(j, i):
                t = 2 * j + i
                pe.wait_ge(evacuated, NQ * (t + 1))
                pe.wait_ge(picked_placed, t + 1)
                for k in range(BLOCKS):
                    if i == 1 or k > 1:
                        pe.wait_ge(gram_copied, BLOCKS * t + max(k - 1, 0))
                    for g in range(BLOCK):
                        s = GROUP * (BLOCK * k + g)
                        bank, r = divmod(g, GROUPS_PER_BANK)
                        last = nc.tensor.matmul(
                            gram_ps[k % 2][:, bank, r * GROUP * NF:(r + 1) * GROUP * NF],
                            feat_t[:, s:s + GROUP, :], feat_t[:, s:s + GROUP, 0:NF], start=True, stop=True)
                    last.then_inc(gram_done, 1)

            def layers(j, i):
                t = 2 * j + i
                pe.wait_ge(dense_t_made, t + 1)
                pe.wait_ge(pairs_read[i], 16 * KC * (j + 1))
                for n in range(N1):
                    cols = slice(n * P, (n + 1) * P)
                    nc.tensor.matmul(h1_ps[:, cols], w_dense_sum[:, cols], dense_t[i][:], start=True, stop=False)
                    for c in range(KC):
                        last = nc.tensor.matmul(h1_ps[:, cols], w_pairs_sb[:, c, cols], pairs[i][:, c, :],
                                                start=False, stop=c == KC - 1)
                last.then_inc(layer1_done, 1)
                pe.wait_ge(h1_made, t + 1)
                for m in range(N2):
                    for n in range(N1):
                        last = nc.tensor.matmul(h2_ps[:, m * P:(m + 1) * P], w2_sb[:, n, m * P:(m + 1) * P],
                                                h1[:, n, :], start=n == 0, stop=n == N1 - 1)
                last.then_inc(layer2_done, 1)
                pe.wait_ge(h2_made, t + 1)
                for m in range(N2):
                    last = nc.tensor.matmul(h2_ps[0:1, N2 * P:(N2 + 1) * P], w3_sb[:, m:m + 1], h2[:, m, :],
                                            start=m == 0, stop=m == N2 - 1)
                last.then_inc(layer3_done, 1)

            pick(0, 0)
            pick(0, 1)
            with pe.Fori(1, NP // 2) as kk:
                pick(kk, 0)
                pick(kk, 1)
            pe.wait_ge(picked_copied, NP)
            pe.wait_ge(identity_made, 1)
            pe.wait_ge(pads_zeroed, 1)
            pe.wait_ge(weights_loaded, 16 * N_WEIGHT_DMAS)
            pe.wait_ge(weights_summed, 1)
            with pe.Fori(0, TILES // 2) as j:
                for i in range(2):
                    for q in range(NQ):
                        transpose_quartet(j, i, q)
                    gram_products(j, i)
                for i in range(2):
                    layers(j, i)

        @block.vector
        def _(dve):
            def prepare_pick(kk, i):
                k = 2 * kk + i
                wait_after_first(dve, picked, k - 1)
                dve.wait_ge(wanted_loaded[i], 16 * (kk + 1))
                for c in range(PICK_CHUNKS):
                    dve.tensor_scalar(onehot[i][:, c, :], wanted[i][:], row_number[:, c:c + 1], None,
                                      ALU.is_equal).then_inc(onehot_made, 1)
                dve.wait_ge(hi_made, k + 1)
                dve.tensor_tensor(table_lo[i][:], table[i][:], table_hi[i][:].bitcast(F32), ALU.subtract).then_inc(lo_made, 1)

            def assemble_tile(t, j, i):
                wait_after_first(dve, dense_t_made, t)
                wait_after_first(dve, gram_done, BLOCKS * t)
                dve.tensor_copy(feat_t[:, :, SLOTS:NF].rearrange("d s f -> d f s"),
                                picked_t[:, :, bass.ds(t * P, P)]).then_inc(picked_placed, 1)
                for q, slots in enumerate(QUARTETS):
                    dve.wait_ge(transposed[q], t + 1)
                    dve.tensor_copy(feat_t[:, :, slots[0]:slots[-1] + 1].rearrange("d s f -> d f s"),
                                    transposed_ps[q % 2][:, 0:len(slots), :]).then_inc(evacuated, 1)
                dve.wait_ge(evacuated, NQ * t + 1)
                dve.tensor_copy(dense_t[i][:], feat_t[:, :, 0]).then_inc(dense_t_made, 1)

            dve.memset(feat_t[:, :, NF:QUAD], 0.0).then_inc(pads_zeroed, 1)
            dve.wait_ge(row_number_made, 1)
            prepare_pick(0, 0)
            prepare_pick(0, 1)
            with dve.Fori(1, NP // 2) as kk:
                prepare_pick(kk, 0)
                prepare_pick(kk, 1)
            dve.wait_ge(weights_loaded, 16 * N_WEIGHT_DMAS)
            dve.tensor_tensor(w_dense_sum[:], w_dense_sb[:, 0, :], w_dense_sb[:, 1, :], ALU.add).then_inc(weights_summed, 1)
            dve.wait_ge(picked_copied, NP)
            assemble_tile(0, 0, 0)
            assemble_tile(1, 0, 1)
            with dve.Fori(1, TILES // 2) as j:
                assemble_tile(2 * j, j, 0)
                assemble_tile(2 * j + 1, j, 1)

        @block.scalar
        def _(act):
            def high_part(kk, i):
                act.wait_ge(table_loaded[i], 16 * (kk + 1))
                nc.scalar.copy(table_hi[i][:], table[i][:]).then_inc(hi_made, 1)

            def copy_picked(k, i):
                act.wait_ge(picked, k + 1)
                nc.scalar.copy(picked_t[:, bass.ds(k, 1), :], picked_ps[i][:]).then_inc(picked_copied, 1)

            def copy_gram(j, i):
                t = 2 * j + i
                if i == 1:
                    act.wait_ge(gram_written, 32 * t)
                for k in range(BLOCKS):
                    act.wait_ge(gram_done, BLOCKS * t + k + 1)
                    ps = gram_ps[k % 2][:, :, 0:GROUPS_PER_BANK * GROUP * NF].rearrange(
                        "p b (r s g) -> p b r s g", r=GROUPS_PER_BANK, s=GROUP)
                    to = gram[:, :, GROUP * BLOCK * k:GROUP * BLOCK * (k + 1)].rearrange(
                        "f g (b r s) -> f b r s g", b=BLOCK_BANKS, s=GROUP)
                    for s in range(GROUP):
                        last = nc.scalar.copy(to[:, :, :, s, :], ps[QUAD * s:QUAD * s + NF, :, :, s, :])
                    last.then_inc(gram_copied, 1)

            def activations(j, i):
                t = 2 * j + i
                act.wait_ge(layer1_done, t + 1)
                for n in range(N1):
                    last = nc.scalar.activation(h1[:, n, :], h1_ps[:, n * P:(n + 1) * P], ACT.Relu, bias=b1_sb[:, n:n + 1])
                last.then_inc(h1_made, 1)
                act.wait_ge(layer2_done, t + 1)
                for m in range(N2):
                    last = nc.scalar.activation(h2[:, m, :], h2_ps[:, m * P:(m + 1) * P], ACT.Relu, bias=b2_sb[:, m:m + 1])
                last.then_inc(h2_made, 1)
                act.wait_ge(layer3_done, t + 1)
                nc.scalar.copy(y_all[:, bass.ds(t * P, P)], h2_ps[0:1, N2 * P:(N2 + 1) * P]).then_inc(y_made, 1)

            high_part(0, 0)
            high_part(0, 1)
            with act.Fori(0, NP // 2 - 1) as kk:
                for i in range(2):
                    copy_picked(2 * kk + i, i)
                    high_part(kk + 1, i)
            copy_picked(NP - 2, 0)
            copy_picked(NP - 1, 1)
            act.wait_ge(weights_loaded, 16 * N_WEIGHT_DMAS)
            with act.Fori(0, TILES // 2) as j:
                for i in range(2):
                    copy_gram(j, i)
                for i in range(2):
                    activations(j, i)


def kernel(**inputs):
    import numpy as np
    import concourse.bacc as bacc
    from concourse.bass_utils import run_bass_kernel_spmd

    ids = np.asarray(inputs["ids"])
    dense = np.ascontiguousarray(inputs["r_dense_features"])
    B, NS = ids.shape
    D = dense.shape[1]
    NF = NS + 1
    ND = (NF - 1) // 2
    KC = 3
    tables = [np.asarray(inputs[f"tbl_{n}"]) for n in range(NS)]
    picked = [n for n in range(NS) if tables[n].shape[0] == 1000][:MAX_PICKED]
    gathered = [n for n in range(NS) if n not in picked]
    feature = np.array([0] + [n + 1 for n in gathered + picked])
    first, second = np.triu_indices(NF, k=1)
    row_of = np.zeros((NF, NF), np.int64)
    row_of[first, second] = row_of[second, first] = D + np.arange(len(first))
    f = np.arange(NF)[:, None]
    order = row_of[feature[f], feature[(f + 1 + np.arange(ND)[None, :]) % NF]].reshape(KC, -1)
    w1 = np.asarray(inputs["W_top1"])
    arrays = {
        "dense": dense,
        "ids": np.ascontiguousarray(ids[:, gathered]),
        "pick_ids": np.ascontiguousarray(ids[:, picked].T),
        "pick_tables": np.stack([tables[n] for n in picked]),
        "w_pairs": np.ascontiguousarray(w1[order].transpose(1, 0, 2)),
        "w_dense": np.ascontiguousarray(np.stack([w1[:D], w1[D + len(first):]], axis=1)),
        "b1": np.ascontiguousarray(np.asarray(inputs["b_top1"]).reshape(-1, P).T),
        "w2": np.ascontiguousarray(inputs["W_top2"]),
        "b2": np.ascontiguousarray(np.asarray(inputs["b_top2"]).reshape(-1, P).T),
        "w3": np.ascontiguousarray(np.asarray(inputs["W_top3"]).reshape(-1, P).T),
    }
    for n in gathered:
        arrays[f"tbl_{n}"] = np.ascontiguousarray(tables[n])

    nc = bacc.Bacc("TRN2", target_bir_lowering=False, num_devices=1)
    ap = {n: nc.dram_tensor(n, a.shape, mybir.dt.from_np(a.dtype), kind="ExternalInput").ap()
          for n, a in arrays.items()}
    out = nc.dram_tensor("out", (1, B), F32, kind="ExternalOutput").ap()
    dlrm_tower(nc, ap["dense"], ap["ids"], ap["pick_ids"], ap["pick_tables"], [ap[f"tbl_{n}"] for n in gathered],
               ap["w_pairs"], ap["w_dense"], ap["b1"], ap["w2"], ap["b2"], ap["w3"], out)
    result = run_bass_kernel_spmd(nc, [arrays], core_ids=[0])
    return result.results[0]["out"].reshape(B, 1)
```

```python
from contextlib import ExitStack

import concourse.bass as bass
from concourse import mybir

F32 = mybir.dt.float32
F32R = mybir.dt.float32r
I32 = mybir.dt.int32
ALU = mybir.AluOpType
ACT = mybir.ActivationFunctionType

P = 128
QUAD = 32
QUADS = P // QUAD
BLOCKS = 2
SMALL = 6
T_PER_BANK = 4
WARM_UP = 11
T_BANKS = 2
PICK_CHUNKS = 8
DVE_CHUNKS = 6
MAX_PICKED = 9


def dlrm_tower(nc, dense, ids, pick_ids, pick_tables, tables, w_pairs, w_dense, b1, w2, b2, w3, out):
    D, B = dense.shape
    NG = len(tables)
    NT, V, _ = pick_tables.shape
    NP = NT - 1
    PV = V // PICK_CHUNKS
    NF = NG + 1 + NP
    ND = (NF - 1) // 2
    KP, KC, H1 = w_pairs.shape
    FC = NF // KC
    NW = FC + ND - 1
    H2 = w2.shape[1]
    N1, N2 = H1 // P, H2 // P
    NH = N1 // 2
    TILES = B // P
    NQ = -(-NG // T_PER_BANK)
    RUN = P // QUADS // BLOCKS
    assert D == P and B == 512 and NF % 2 == 1 and NF <= QUAD and KP == FC * ND and RUN * QUAD == 512
    assert V % PICK_CHUNKS == 0 and PV <= P and NP % 2 == 1 and NP >= 5
    assert TILES == 4 and NQ == 5 and N1 % 2 == 0 and N2 == 2

    gram_dram = [[nc.dram_tensor(f"gram_dram{i}_{c}", (FC, NW, P), F32, kind="Internal").ap() for c in range(KC)]
                 for i in range(2)]

    with ExitStack() as ctx:
        def sb(name, shape, dt=F32):
            return ctx.enter_context(nc.sbuf_tensor(name, shape, dt))

        def psum(name, shape):
            return ctx.enter_context(nc.psum_tensor(name, shape, F32))

        def sem(name):
            return ctx.enter_context(nc.semaphore(name))

        table = [sb(f"table{i}", [PV, PICK_CHUNKS, D]) for i in range(2)]
        table_hi = [sb(f"table_hi{i}", [PV, PICK_CHUNKS, D], F32R) for i in range(2)]
        table_lo = [sb(f"table_lo{i}", [PV, PICK_CHUNKS, D], F32R) for i in range(2)]
        wanted = sb("wanted", [PV, NP + 1, B], I32)
        row_number = sb("row_number", [PV, PICK_CHUNKS])
        distance = sb("distance", [PV, PICK_CHUNKS - DVE_CHUNKS, B])
        row_negated = sb("row_negated", [PV, PICK_CHUNKS])
        onehot = [sb(f"onehot{i}", [PV, PICK_CHUNKS, B], F32R) for i in range(2)]
        columns_t = sb("columns_t", [P, 1 + NP, B])
        shared_t = sb("shared_t", [P, B // 2])
        ids_sb = sb("ids_sb", [P, TILES, NG], I32)
        rows = [sb(f"rows{i}", [P, NG, D]) for i in range(2)]
        identity = sb("identity", [P, P])
        feat_t = [sb(f"feat_t{i}", [P, P, QUAD]) for i in range(2)]
        gram = [sb(f"gram{i}", [NF, NF, P]) for i in range(2)]
        pairs = [sb(f"pairs{i}", [KP, KC, P]) for i in range(2)]
        w_pairs_sb = sb("w_pairs_sb", [KP, KC, H1])
        w_dense_sb = sb("w_dense_sb", [P, 2, H1])
        w_dense_sum = sb("w_dense_sum", [P, H1])
        w2_sb = sb("w2_sb", [P, N1, H2])
        w3_sb = sb("w3_sb", [P, N2])
        b1_sb = sb("b1_sb", [P, N1])
        b2_sb = sb("b2_sb", [P, N2])
        h1 = [sb(f"h1_{i}", [P, N1, P]) for i in range(2)]
        h2 = [sb(f"h2_{i}", [P, N2, P]) for i in range(2)]
        y_all = sb("y_all", [1, B])

        transposed_ps = [psum(f"transposed_ps{i}", [P, T_PER_BANK, P]) for i in range(T_BANKS)]
        last_gram_ps = transposed_ps[0][:].rearrange("p n s -> p (n s)")
        gram_ps = [psum(f"gram_ps{k}", [P, 512]) for k in range(BLOCKS)]
        h1_ps = [psum(f"h1_ps{i}", [P, B]) for i in range(2)]
        h2_ps = [psum(f"h2_ps{i}", [P, 2, P]) for i in range(2)]
        picked_ps = h1_ps

        table_loaded = [sem(f"table_loaded{i}") for i in range(2)]
        first_wanted_loaded = [sem(f"first_wanted_loaded{k}") for k in range(2)]
        wanted_loaded = sem("wanted_loaded")
        row_number_made = sem("row_number_made")
        hi_made = sem("hi_made")
        lo_made = sem("lo_made")
        onehot_made_dve = sem("onehot_made_dve")
        row_negated_made = sem("row_negated_made")
        distance_made = sem("distance_made")
        onehot_made_act = sem("onehot_made_act")
        picked = sem("picked")
        picked_copied = sem("picked_copied")
        columns_placed = sem("columns_placed")
        ids_loaded = sem("ids_loaded")
        dense_loaded = sem("dense_loaded")
        weights_loaded = sem("weights_loaded")
        identity_zeroed = sem("identity_zeroed")
        identity_made = sem("identity_made")
        gathered = [[sem(f"gathered{i}_{f}") for f in range(NG)] for i in range(2)]
        transposed = sem("transposed")
        evacuated = sem("evacuated")
        pads_zeroed = sem("pads_zeroed")
        weights_summed = sem("weights_summed")
        gram_done = sem("gram_done")
        gram_copied_act = sem("gram_copied_act")
        gram_copied_dve = sem("gram_copied_dve")
        gram_written = [[sem(f"gram_written{i}_{c}") for c in range(KC)] for i in range(2)]
        pairs_read = [[sem(f"pairs_read{i}_{c}") for c in range(KC)] for i in range(2)]
        layer1_done = [sem(f"layer1_done{half}") for half in range(2)]
        layer2_done = [sem(f"layer2_done{half}") for half in range(2)]
        layer3_done = sem("layer3_done")
        h1_made_act = sem("h1_made_act")
        h1_made_dve = sem("h1_made_dve")
        h2_made_act = sem("h2_made_act")
        h2_made_dve = sem("h2_made_dve")
        y_made = sem("y_made")
        out_written = sem("out_written")

        def wait_after_first(engine, semaphore, count):
            if not isinstance(count, int) or count > 0:
                engine.wait_ge(semaphore, count)

        def gathered_features(t):
            return NG if t < TILES // 2 else NG - 1

        def quartet(t, q):
            n = gathered_features(t)
            return range(T_PER_BANK * q, min(T_PER_BANK * (q + 1), n - 1)) if q < NQ - 1 else range(n - 1, n)

        def picked_samples(kk, i):
            return slice(B // 2 if isinstance(kk, int) and 2 * kk + i == NP else 0, B)

        def placings(t):
            return t + 2 + max(0, t - TILES // 2 + 1)

        def wait_wanted(engine, kk, i):
            if isinstance(kk, int) and kk == 0:
                engine.wait_ge(first_wanted_loaded[i], 16)
            elif i == 0:
                engine.wait_ge(wanted_loaded, 16 * kk)

        def dve_chunks(kk, i):
            return PICK_CHUNKS if isinstance(kk, int) and kk == 0 and i == 0 else DVE_CHUNKS

        def onehots_of_dve(kk, i, c):
            k = 2 * kk + i
            return c + 1 if isinstance(k, int) and k == 0 else DVE_CHUNKS * k + (PICK_CHUNKS - DVE_CHUNKS) + c + 1

        def blocks(t):
            if t < TILES - 1:
                return [(gram_ps[k], RUN * k, RUN) for k in range(BLOCKS)]
            return [(gram_ps[0], 0, RUN), (gram_ps[1], RUN, RUN - SMALL), (last_gram_ps, QUAD - SMALL, SMALL)]

        def gram_copy(t, k, j):
            bank, first, count = blocks(t)[k]
            source = bank[QUAD * j:QUAD * j + NF, 0:QUAD * count].rearrange("f (r g) -> f g r", g=QUAD)[:, 0:NF, :]
            return gram[t % 2][:, :, QUAD * j + first:QUAD * j + first + count], source

        block = ctx.enter_context(nc.Block())
        N_WEIGHT_DMAS = 6

        @block.sync
        def _(sp):
            def load_table(kk, i):
                k = 2 * kk + i
                wait_after_first(sp, lo_made, k - 1)
                sp.dma_start(table[i][:], pick_tables[bass.ds(k, 1), :, :].rearrange(
                    "o (p c) d -> p (o c) d", c=PICK_CHUNKS)).then_inc(table_loaded[i], 16)

            def load_first_wanted(k):
                sp.dma_start(wanted[:, k, :], pick_ids[k:k + 1, :].to_broadcast([PV, B])).then_inc(first_wanted_loaded[k], 16)

            def load_wanted(kk):
                wait_after_first(sp, wanted_loaded, 16 * (kk - 1))
                sp.dma_start(wanted[:, bass.ds(2 * kk, 2), :], pick_ids[bass.ds(2 * kk, 2), :].unsqueeze(0).to_broadcast(
                    [PV, 2, B])).then_inc(wanted_loaded, 16)

            def write_gram(t, c):
                i, rows_f, first = t % 2, slice(FC * c, FC * (c + 1)), FC * c + 1
                end = min(first + NW, NF)
                sp.dma_start(gram_dram[i][c][:, 0:end - first, :], gram[i][rows_f, first:end, :]).then_inc(gram_written[i][c], 16)
                if first + NW > NF:
                    sp.dma_start(gram_dram[i][c][:, NF - first:, :], gram[i][rows_f, 0:first + NW - NF, :]).then_inc(
                        gram_written[i][c], 16)

            sp.dma_start(ids_sb[:], ids.rearrange("(t p) f -> p t f", p=P)).then_inc(ids_loaded, 16)
            load_first_wanted(0)
            load_table(0, 0)
            load_table(0, 1)
            load_first_wanted(1)
            load_wanted(1)
            sp.dma_start(columns_t[:, 0, :], dense).then_inc(dense_loaded, 16)
            with sp.Fori(1, NP // 2 - 1) as kk:
                load_table(kk, 0)
                load_table(kk, 1)
                load_wanted(kk + 1)
            load_table(NP // 2 - 1, 0)
            load_table(NP // 2 - 1, 1)
            load_wanted(NP // 2)
            load_table(NP // 2, 0)
            load_table(NP // 2, 1)
            sp.dma_start(w_pairs_sb[:], w_pairs).then_inc(weights_loaded, 16)
            sp.dma_start(w_dense_sb[:], w_dense).then_inc(weights_loaded, 16)
            sp.dma_start(w2_sb[:], w2.rearrange("(c p) n -> p c n", p=P)).then_inc(weights_loaded, 16)
            sp.dma_start(w3_sb[:], w3).then_inc(weights_loaded, 16)
            sp.dma_start(b1_sb[:], b1).then_inc(weights_loaded, 16)
            sp.dma_start(b2_sb[:], b2).then_inc(weights_loaded, 16)
            for t in range(TILES):
                i = t % 2
                sp.wait_ge(gram_copied_act, BLOCKS * t + len(blocks(t)))
                sp.wait_ge(gram_copied_dve, BLOCKS * t + len(blocks(t)))
                for c in range(KC):
                    write_gram(t, c)
                for c in range(KC):
                    sp.wait_ge(gram_written[i][c], (16 if c == 0 else 32) * (t // 2 + 1))
                    src = bass.AP(tensor=gram_dram[i][c].tensor, offset=gram_dram[i][c].offset,
                                  ap=[[(NW + 1) * P, FC], [P, ND], [1, P]])
                    sp.dma_start(pairs[i][:, c, :], src).then_inc(pairs_read[i][c], 16)
            sp.wait_ge(y_made, TILES)
            sp.dma_start(out, y_all[:]).then_inc(out_written, 16)
            sp.wait_ge(out_written, 16)

        @block.gpsimd
        def _(pool):
            pool.iota(row_number[:], [[1, PICK_CHUNKS]], base=0, channel_multiplier=PICK_CHUNKS,
                      allow_small_or_imprecise_dtypes=True).then_inc(row_number_made, 1)
            pool.memset(identity[:], 0.0).then_inc(identity_zeroed, 1)
            pool.wait_ge(identity_zeroed, 1)
            pool.affine_select(out=identity[:], in_=identity[:], compare_op=ALU.not_equal, fill=1.0, base=0,
                               pattern=[[-1, P]], channel_multiplier=1).then_inc(identity_made, 1)
            pool.wait_ge(ids_loaded, 16)
            for t in range(TILES):
                for f in range(gathered_features(t)):
                    if t > 1 and f % T_PER_BANK == 0:
                        pool.wait_ge(transposed, NQ * (t - 2) + f // T_PER_BANK + 1)
                    pool.indirect_dma_start(
                        rows[t % 2][:, f, :], None, tables[f],
                        bass.IndirectOffsetOnAxis(ap=ids_sb[:, t, f:f + 1], axis=0)).then_inc(gathered[t % 2][f], 16)


        @block.tensor
        def _(pe):
            def pick_chunks(kk, i, part, chunks):
                samples = picked_samples(kk, i)
                for c in chunks:
                    last = nc.tensor.matmul(picked_ps[i][:, samples], part[i][:, c, :], onehot[i][:, c, samples],
                                            start=part is table_hi and c == 0,
                                            stop=part is table_lo and c == PICK_CHUNKS - 1)
                return last

            def pick_begin(kk, i):
                k = 2 * kk + i
                wait_after_first(pe, picked_copied, k - 1)
                pe.wait_ge(hi_made, k + 1)
                for c in range(dve_chunks(kk, i)):
                    pe.wait_ge(onehot_made_dve, onehots_of_dve(kk, i, c))
                    pick_chunks(kk, i, table_hi, [c])

            def pick_end(kk, i):
                k = 2 * kk + i
                pe.wait_ge(lo_made, k + 1)
                n = dve_chunks(kk, i)
                last = pick_chunks(kk, i, table_lo, range(n))
                if n < PICK_CHUNKS:
                    pe.wait_ge(onehot_made_act, k)
                    pick_chunks(kk, i, table_hi, range(n, PICK_CHUNKS))
                    last = pick_chunks(kk, i, table_lo, range(n, PICK_CHUNKS))
                last.then_inc(picked, 1)

            def transpose_quartet(t, q):
                m = NQ * t + q
                if m >= T_BANKS:
                    pe.wait_ge(evacuated, m - T_BANKS + 1)
                for n, f in enumerate(quartet(t, q)):
                    pe.wait_ge(gathered[t % 2][f], 16 * (t // 2 + 1))
                    last = nc.tensor.transpose(transposed_ps[m % T_BANKS][:, n, :], rows[t % 2][:, f, :], identity[:])
                last.then_inc(transposed, 1)

            def gram_products(t, k):
                if k == 0:
                    pe.wait_ge(evacuated, NQ * (t + 1))
                    pe.wait_ge(columns_placed, placings(t))
                bank, first, count = blocks(t)[k]
                if t > 0 and k < BLOCKS:
                    pe.wait_ge(gram_copied_act, BLOCKS * (t - 1) + k + 1)
                    pe.wait_ge(gram_copied_dve, BLOCKS * (t - 1) + k + 1)
                for r in range(count):
                    for j in range(QUADS):
                        sample = QUAD * j + first + r
                        last = nc.tensor.matmul(
                            bank[QUAD * j:QUAD * (j + 1), r * QUAD:(r + 1) * QUAD],
                            feat_t[t % 2][:, sample, :], feat_t[t % 2][:, sample, :],
                            start=True, stop=True, tile_position=(0, QUAD * j))
                last.then_inc(gram_done, 1)

            def layer1_dense(t):
                if t > 0:
                    pe.wait_ge(h1_made_act, NH * t)
                    pe.wait_ge(h1_made_dve, NH * t)
                else:
                    pe.wait_ge(picked_copied, NP + 1)
                pe.wait_ge(dense_loaded, 16)
                for n in range(N1):
                    half, m = divmod(n, NH)
                    nc.tensor.matmul(h1_ps[half][:, m * P:(m + 1) * P], w_dense_sum[:, n * P:(n + 1) * P],
                                     columns_t[:, 0, t * P:(t + 1) * P], start=m == 0, stop=False, skip_group_check=True)

            def layer1_pairs(t, first=0, end=KC * N1):
                for product in range(first, end):
                    c, n = divmod(product, N1)
                    half, m = divmod(n, NH)
                    if n == 0:
                        pe.wait_ge(pairs_read[t % 2][c], 16 * (t // 2 + 1))
                    last = nc.tensor.matmul(h1_ps[half][:, m * P:(m + 1) * P], w_pairs_sb[:, c, n * P:(n + 1) * P],
                                            pairs[t % 2][:, c, :], start=False, stop=c == KC - 1, skip_group_check=True)
                    if c == KC - 1 and m == NH - 1:
                        last.then_inc(layer1_done[half], 1)

            def layer2_half(t, m):
                if t > 0:
                    pe.wait_ge(h2_made_dve if m else y_made, t)
                for n in range(N1):
                    if m == 0:
                        half, mm = divmod(n, NH)
                        pe.wait_ge(h1_made_dve if half else h1_made_act, NH * t + mm + 1)
                    last = nc.tensor.matmul(h2_ps[m][:, 0, :], w2_sb[:, n, m * P:(m + 1) * P], h1[t % 2][:, n, :],
                                            start=n == 0, stop=n == N1 - 1)
                last.then_inc(layer2_done[m], 1)

            def layer3(t):
                for m in range(N2):
                    pe.wait_ge(h2_made_dve if m else h2_made_act, t + 1)
                    last = nc.tensor.matmul(h2_ps[0][0:1, 1, :], w3_sb[:, m:m + 1], h2[t % 2][:, m, :],
                                            start=m == 0, stop=m == N2 - 1)
                last.then_inc(layer3_done, 1)

            pe.wait_ge(identity_made, 1)
            for _ in range(WARM_UP):
                nc.tensor.matmul(gram_ps[0][:, 0:P], identity[:], identity[:], start=True, stop=True)
            for i in range(2):
                pick_begin(0, i)
                pick_end(0, i)
            transpose_quartet(0, 0)
            transpose_quartet(0, 1)
            with pe.Fori(1, NP // 2) as kk:
                for i in range(2):
                    pick_begin(kk, i)
                    pick_end(kk, i)
            transpose_quartet(0, 2)
            transpose_quartet(0, 3)
            for i in range(2):
                pick_begin(NP // 2, i)
                pick_end(NP // 2, i)
            transpose_quartet(0, 4)
            transpose_quartet(1, 0)
            transpose_quartet(1, 1)
            pe.wait_ge(pads_zeroed, 2)
            gram_products(0, 0)
            transpose_quartet(1, 2)
            transpose_quartet(1, 3)
            gram_products(0, 1)
            transpose_quartet(1, 4)
            transpose_quartet(2, 0)
            pe.wait_ge(weights_loaded, 16 * N_WEIGHT_DMAS)
            pe.wait_ge(weights_summed, 1)
            layer1_dense(0)
            gram_products(1, 0)
            transpose_quartet(2, 1)
            transpose_quartet(2, 2)
            gram_products(1, 1)
            transpose_quartet(2, 3)
            layer1_pairs(0)
            transpose_quartet(2, 4)
            layer2_half(0, 0)
            layer2_half(0, 1)
            gram_products(2, 0)
            layer3(0)
            transpose_quartet(3, 0)
            gram_products(2, 1)
            transpose_quartet(3, 1)
            layer1_dense(1)
            layer1_pairs(1)
            transpose_quartet(3, 2)
            layer2_half(1, 0)
            layer2_half(1, 1)
            transpose_quartet(3, 3)
            layer3(1)
            layer1_dense(2)
            transpose_quartet(3, 4)
            layer1_pairs(2, 0, 2)
            for k in range(len(blocks(3))):
                gram_products(3, k)
            layer1_pairs(2, 2)
            layer2_half(2, 0)
            layer2_half(2, 1)
            layer1_dense(3)
            layer3(2)
            layer1_pairs(3)
            layer2_half(3, 0)
            layer2_half(3, 1)
            layer3(3)

        @block.vector
        def _(dve):
            def prepare_pick(kk, i):
                k = 2 * kk + i
                wait_after_first(dve, picked, k - 1)
                wait_wanted(dve, kk, i)
                samples = picked_samples(kk, i)
                for c in range(dve_chunks(kk, i)):
                    dve.tensor_scalar(onehot[i][:, c, samples], wanted[:, bass.ds(k, 1), samples], row_number[:, c:c + 1], None,
                                      ALU.is_equal).then_inc(onehot_made_dve, 1)
                dve.wait_ge(hi_made, k + 1)
                dve.tensor_tensor(table_lo[i][:], table[i][:], table_hi[i][:].bitcast(F32), ALU.subtract).then_inc(lo_made, 1)

            def place_columns(t, first=0, end=1 + NP):
                dve.tensor_copy(feat_t[t % 2][:, :, NG + first:NG + end].rearrange("d s f -> d f s"),
                                columns_t[:, first:end, t * P:(t + 1) * P]).then_inc(columns_placed, 1)

            def place_shared(t):
                first = (t - TILES // 2) * P
                dve.tensor_copy(feat_t[t % 2][:, :, NG - 1], shared_t[:, first:first + P]).then_inc(columns_placed, 1)

            def free_features(t):
                dve.wait_ge(gram_done, BLOCKS * (t - 1))

            def evacuate(t, q):
                m, features = NQ * t + q, quartet(t, q)
                dve.wait_ge(transposed, m + 1)
                dve.tensor_copy(feat_t[t % 2][:, :, features[0]:features[-1] + 1].rearrange("d s f -> d f s"),
                                transposed_ps[m % T_BANKS][:, 0:len(features), :]).then_inc(evacuated, 1)

            def copy_gram(t, k):
                dve.wait_ge(gram_done, BLOCKS * t + k + 1)
                for j in range(QUADS // 2, QUADS):
                    last = dve.tensor_copy(*gram_copy(t, k, j))
                last.then_inc(gram_copied_dve, 1)

            def relu1(t):
                dve.wait_ge(layer1_done[1], t + 1)
                for n in range(NH, N1):
                    dve.tensor_scalar(h1[t % 2][:, n, :], h1_ps[1][:, (n - NH) * P:(n - NH + 1) * P],
                                      b1_sb[:, n:n + 1], 0.0, ALU.add, ALU.max).then_inc(h1_made_dve, 1)

            def relu2(t):
                dve.wait_ge(layer2_done[1], t + 1)
                dve.tensor_scalar(h2[t % 2][:, 1, :], h2_ps[1][:, 0, :], b2_sb[:, 1:2], 0.0,
                                  ALU.add, ALU.max).then_inc(h2_made_dve, 1)

            for i in range(2):
                dve.memset(feat_t[i][:, :, NF:QUAD], 0.0).then_inc(pads_zeroed, 1)
            dve.wait_ge(row_number_made, 1)
            prepare_pick(0, 0)
            prepare_pick(0, 1)
            with dve.Fori(1, NP // 2) as kk:
                prepare_pick(kk, 0)
                prepare_pick(kk, 1)
            evacuate(0, 0)
            evacuate(0, 1)
            prepare_pick(NP // 2, 0)
            prepare_pick(NP // 2, 1)
            evacuate(0, 2)
            evacuate(0, 3)
            dve.wait_ge(dense_loaded, 16)
            dve.wait_ge(picked_copied, NP - 1)
            place_columns(0, 0, NP)
            evacuate(0, 4)
            dve.wait_ge(picked_copied, NP)
            place_columns(0, NP)
            evacuate(1, 0)
            evacuate(1, 1)
            place_columns(1)
            dve.wait_ge(weights_loaded, 16 * N_WEIGHT_DMAS)
            dve.tensor_tensor(w_dense_sum[:], w_dense_sb[:, 0, :], w_dense_sb[:, 1, :], ALU.add).then_inc(weights_summed, 1)
            copy_gram(0, 0)
            evacuate(1, 2)
            evacuate(1, 3)
            copy_gram(0, 1)
            evacuate(1, 4)
            free_features(2)
            evacuate(2, 0)
            place_columns(2)
            dve.wait_ge(picked_copied, NP + 1)
            place_shared(2)
            copy_gram(1, 0)
            evacuate(2, 1)
            evacuate(2, 2)
            copy_gram(1, 1)
            evacuate(2, 3)
            relu1(0)
            evacuate(2, 4)
            relu2(0)
            free_features(3)
            place_columns(3)
            place_shared(3)
            copy_gram(2, 0)
            evacuate(3, 0)
            copy_gram(2, 1)
            evacuate(3, 1)
            relu1(1)
            evacuate(3, 2)
            relu2(1)
            evacuate(3, 3)
            evacuate(3, 4)
            for k in range(len(blocks(3))):
                copy_gram(3, k)
            relu1(2)
            relu2(2)
            relu1(3)
            relu2(3)

        @block.scalar
        def _(act):
            def high_part(kk, i):
                act.wait_ge(table_loaded[i], 16 * (kk + 1))
                nc.scalar.copy(table_hi[i][:], table[i][:]).then_inc(hi_made, 1)

            def make_onehot(kk, i):
                k = 2 * kk + i
                wait_after_first(act, onehot_made_act, k - 1)
                wait_wanted(act, kk, i)
                samples = picked_samples(kk, i)
                for c in range(DVE_CHUNKS, PICK_CHUNKS):
                    last = nc.scalar.activation(distance[:, c - DVE_CHUNKS, samples], wanted[:, bass.ds(k, 1), samples], ACT.Abs,
                                                bias=row_negated[:, c:c + 1])
                last.then_inc(distance_made, 1)
                act.wait_ge(distance_made, k)
                nc.scalar.activation(onehot[i][:, DVE_CHUNKS:, samples], distance[:, :, samples], ACT.Relu, bias=1.0,
                                     scale=-1.0).then_inc(onehot_made_act, 1)

            def copy_picked(k, i):
                act.wait_ge(picked, k + 1)
                nc.scalar.copy(columns_t[:, bass.ds(k + 1, 1), :], picked_ps[i][:]).then_inc(picked_copied, 1)

            def copy_gram(t, k):
                act.wait_ge(gram_done, BLOCKS * t + k + 1)
                for j in range(QUADS // 2):
                    last = nc.scalar.copy(*gram_copy(t, k, j))
                last.then_inc(gram_copied_act, 1)

            def relu1(t):
                act.wait_ge(layer1_done[0], t + 1)
                for n in range(NH):
                    nc.scalar.activation(h1[t % 2][:, n, :], h1_ps[0][:, n * P:(n + 1) * P], ACT.Relu,
                                         bias=b1_sb[:, n:n + 1]).then_inc(h1_made_act, 1)

            def relu2(t):
                act.wait_ge(layer2_done[0], t + 1)
                nc.scalar.activation(h2[t % 2][:, 0, :], h2_ps[0][:, 0, :], ACT.Relu, bias=b2_sb[:, 0:1]).then_inc(h2_made_act, 1)

            def copy_y(t):
                act.wait_ge(layer3_done, t + 1)
                nc.scalar.copy(y_all[:, t * P:(t + 1) * P], h2_ps[0][0:1, 1, :]).then_inc(y_made, 1)

            act.wait_ge(row_number_made, 1)
            nc.scalar.activation(row_negated[:], row_number[:], ACT.Copy,
                                 scale=-1.0).then_inc(row_negated_made, 1)
            act.wait_ge(row_negated_made, 1)
            high_part(0, 0)
            high_part(0, 1)
            make_onehot(0, 1)
            with act.Fori(0, NP // 2 - 1) as kk:
                for i in range(2):
                    copy_picked(2 * kk + i, i)
                    high_part(kk + 1, i)
                    make_onehot(kk + 1, i)
            copy_picked(NP - 3, 0)
            high_part(NP // 2, 0)
            make_onehot(NP // 2, 0)
            copy_picked(NP - 2, 1)
            high_part(NP // 2, 1)
            make_onehot(NP // 2, 1)
            copy_picked(NP - 1, 0)
            act.wait_ge(picked, NP + 1)
            nc.scalar.copy(shared_t[:], picked_ps[1][:, picked_samples(NP // 2, 1)]).then_inc(picked_copied, 1)
            act.wait_ge(weights_loaded, 16 * N_WEIGHT_DMAS)
            for t in range(2):
                for k in range(BLOCKS):
                    copy_gram(t, k)
            relu1(0)
            relu2(0)
            copy_gram(2, 0)
            copy_y(0)
            copy_gram(2, 1)
            relu1(1)
            relu2(1)
            copy_y(1)
            for k in range(len(blocks(3))):
                copy_gram(3, k)
            relu1(2)
            relu2(2)
            copy_y(2)
            relu1(3)
            relu2(3)
            copy_y(3)


def kernel(**inputs):
    import numpy as np
    import concourse.bacc as bacc
    from concourse.bass_utils import run_bass_kernel_spmd

    ids = np.asarray(inputs["ids"])
    dense = np.ascontiguousarray(np.asarray(inputs["r_dense_features"]).T)
    B, NS = ids.shape
    D = dense.shape[0]
    NF = NS + 1
    ND = (NF - 1) // 2
    KC = 3
    tables = [np.asarray(inputs[f"tbl_{n}"]) for n in range(NS)]
    small = [n for n in range(NS) if tables[n].shape[0] == 1000]
    picked, shared = small[:MAX_PICKED], small[MAX_PICKED]
    gathered = [n for n in range(NS) if n not in picked and n != shared] + [shared]
    feature = np.array([n + 1 for n in gathered] + [0] + [n + 1 for n in picked])
    first, second = np.triu_indices(NF, k=1)
    row_of = np.zeros((NF, NF), np.int64)
    row_of[first, second] = row_of[second, first] = D + np.arange(len(first))
    f = np.arange(NF)[:, None]
    order = row_of[feature[f], feature[(f + 1 + np.arange(ND)[None, :]) % NF]].reshape(KC, -1)
    w1 = np.asarray(inputs["W_top1"])
    arrays = {
        "dense": dense,
        "ids": np.ascontiguousarray(ids[:, gathered]),
        "pick_ids": np.ascontiguousarray(ids[:, picked + [shared]].T),
        "pick_tables": np.stack([tables[n] for n in picked + [shared]]),
        "w_pairs": np.ascontiguousarray(w1[order].transpose(1, 0, 2)),
        "w_dense": np.ascontiguousarray(np.stack([w1[:D], w1[D + len(first):]], axis=1)),
        "b1": np.ascontiguousarray(np.asarray(inputs["b_top1"]).reshape(-1, P).T),
        "w2": np.ascontiguousarray(inputs["W_top2"]),
        "b2": np.ascontiguousarray(np.asarray(inputs["b_top2"]).reshape(-1, P).T),
        "w3": np.ascontiguousarray(np.asarray(inputs["W_top3"]).reshape(-1, P).T),
    }
    for n in gathered:
        arrays[f"tbl_{n}"] = np.ascontiguousarray(tables[n])

    nc = bacc.Bacc("TRN2", target_bir_lowering=False, num_devices=1)
    ap = {n: nc.dram_tensor(n, a.shape, mybir.dt.from_np(a.dtype), kind="ExternalInput").ap()
          for n, a in arrays.items()}
    out = nc.dram_tensor("out", (1, B), F32, kind="ExternalOutput").ap()
    dlrm_tower(nc, ap["dense"], ap["ids"], ap["pick_ids"], ap["pick_tables"], [ap[f"tbl_{n}"] for n in gathered],
               ap["w_pairs"], ap["w_dense"], ap["b1"], ap["w2"], ap["b2"], ap["w3"], out)
    result = run_bass_kernel_spmd(nc, [arrays], core_ids=[0])
    return result.results[0]["out"].reshape(B, 1)
```
